# Optimizing a Trainium2 kernel written in Bass

```python
import numpy as np
import jax
import jax.numpy as jnp

def _softmax(x, axis=-1):
    return jax.nn.softmax(x, axis=axis)

def _gelu(x):
    return jax.nn.gelu(x, approximate=True)

def _silu(x):
    return jax.nn.silu(x)

def _sigmoid(x):
    return jax.nn.sigmoid(x)

def _layernorm(x, axis=-1, eps=1e-05):
    m = jnp.mean(x, axis=axis, keepdims=True)
    v = jnp.var(x, axis=axis, keepdims=True)
    return (x - m) / jnp.sqrt(v + eps)

def _scatter_add(tgt, idx, src, axis=0):
    return tgt.at[idx].add(src)

def _segment_sum(src, seg, n):
    return jax.ops.segment_sum(src, seg, n)
kernel_name = 'mk_xattn_seq_d2_seqx_r4_2575f5'

def setup_inputs(seed: int=0):
    np.random.seed(seed)
    _w = jnp.asarray

    def _rec_inputs():
        import jax
        import jax.numpy as jnp
        _rk = jax.random.key(seed)
        x = -0.000125 + 0.9999 * jax.random.normal(jax.random.fold_in(_rk, 1), (16, 256, 512), jnp.float32)
        _lenS = 256 - jax.random.randint(jax.random.fold_in(_rk, 7), (16,), 0, max(1, 256 // 4) + 1, jnp.int32)
        _lenS2 = 256 - jax.random.randint(jax.random.fold_in(_rk, 8), (16,), 0, max(1, 256 // 4) + 1, jnp.int32)
        _ctx_2048P = jax.random.normal(jax.random.fold_in(_rk, 11), (16, 16, 512), jnp.float32)
        _ctx_2048c = jax.random.dirichlet(jax.random.fold_in(_rk, 511), 0.3 * jnp.ones((16,), jnp.float32), (16, 256))
        _ctx_2048t = jnp.einsum('bsk,bkd->bsd', _ctx_2048c, _ctx_2048P)
        _ctx_2048t = _ctx_2048t * jax.lax.rsqrt(jnp.mean(jnp.square(_ctx_2048t)) + 1e-12) * 0.953939
        ctx_2048 = -1.52775e-05 + 0.999936 * (_ctx_2048t + 0.3 * jax.random.normal(jax.random.fold_in(_rk, 611), (16, 256, 512), jnp.float32))
        return (x, ctx_2048)
    x, ctx_2048 = _rec_inputs()

    def _L0_xattn_setup():
        import jax, jax.numpy as jnp
        import numpy as np
        B, C, CI, N = (16, 256, 128, 512)
        EPS = 1e-05

        def _conv1x1(w, b, x):
            return jnp.einsum('oc,bcn->bon', w, x) + b[None, :, None]
        key = jax.random.key(seed)
        ks = jax.random.split(key, 14)
        s = 0.02
        return {'x': jax.random.normal(ks[0], (B, C, N), jnp.float32), 'x_2': jax.random.normal(ks[1], (B, C, N), jnp.float32), 'theta_w': jax.random.normal(ks[2], (CI, C), jnp.float32) * s, 'theta_b': jax.random.normal(ks[3], (CI,), jnp.float32) * s, 'phi_w': jax.random.normal(ks[4], (CI, C), jnp.float32) * s, 'phi_b': jax.random.normal(ks[5], (CI,), jnp.float32) * s, 'g_w': jax.random.normal(ks[6], (CI, C), jnp.float32) * s, 'g_b': jax.random.normal(ks[7], (CI,), jnp.float32) * s, 'w_w': jax.random.normal(ks[8], (C, CI), jnp.float32) * s, 'w_b': jax.random.normal(ks[9], (C,), jnp.float32) * s, 'bn_gamma': jax.random.normal(ks[10], (C,), jnp.float32), 'bn_beta': jax.random.normal(ks[11], (C,), jnp.float32), 'bn_mean': jax.random.normal(ks[12], (C,), jnp.float32), 'bn_var': jax.random.uniform(ks[13], (C,), jnp.float32, 0.5, 1.5)}
    _L0_xattn_all = _L0_xattn_setup()
    _L0_xattn_in = {k: v for k, v in _L0_xattn_all.items() if k in ('theta_w', 'theta_b', 'phi_w', 'phi_b', 'g_w', 'g_b', 'w_w', 'w_b', 'bn_gamma', 'bn_beta', 'bn_mean', 'bn_var')}
    del _L0_xattn_all

    def _L1_xattn_setup():
        import jax, jax.numpy as jnp
        import numpy as np
        B, C1, C2, N = (8, 256, 256, 512)
        D = C2 // 8
        key = jax.random.key(seed)
        ks = jax.random.split(key, 8)
        s1 = 1.0 / np.sqrt(C1)
        s2 = 1.0 / np.sqrt(C2)
        return {'x1': jax.random.normal(ks[0], (B, C1, N), jnp.float32), 'x2': jax.random.normal(ks[1], (B, C2, N), jnp.float32), 'Wq': jax.random.uniform(ks[2], (D, C1), jnp.float32, -s1, s1), 'bq': jax.random.uniform(ks[3], (D,), jnp.float32, -s1, s1), 'Wk': jax.random.uniform(ks[4], (D, C2), jnp.float32, -s2, s2), 'bk': jax.random.uniform(ks[5], (D,), jnp.float32, -s2, s2), 'Wv': jax.random.uniform(ks[6], (C1, C2), jnp.float32, -s2, s2), 'bv': jax.random.uniform(ks[7], (C1,), jnp.float32, -s2, s2)}
    _L1_xattn_all = _L1_xattn_setup()
    _L1_xattn_in = {k: v for k, v in _L1_xattn_all.items() if k in ('Wq', 'bq', 'Wk', 'bk', 'Wv', 'bv')}
    del _L1_xattn_all
    return {'x': x, 'ctx_2048': ctx_2048, 'L0_xattn_theta_w': _L0_xattn_in['theta_w'], 'L0_xattn_theta_b': _L0_xattn_in['theta_b'], 'L0_xattn_phi_w': _L0_xattn_in['phi_w'], 'L0_xattn_phi_b': _L0_xattn_in['phi_b'], 'L0_xattn_g_w': _L0_xattn_in['g_w'], 'L0_xattn_g_b': _L0_xattn_in['g_b'], 'L0_xattn_w_w': _L0_xattn_in['w_w'], 'L0_xattn_w_b': _L0_xattn_in['w_b'], 'L0_xattn_bn_gamma': _L0_xattn_in['bn_gamma'], 'L0_xattn_bn_beta': _L0_xattn_in['bn_beta'], 'L0_xattn_bn_mean': _L0_xattn_in['bn_mean'], 'L0_xattn_bn_var': _L0_xattn_in['bn_var'], 'L1_xattn_Wq': _L1_xattn_in['Wq'], 'L1_xattn_bq': _L1_xattn_in['bq'], 'L1_xattn_Wk': _L1_xattn_in['Wk'], 'L1_xattn_bk': _L1_xattn_in['bk'], 'L1_xattn_Wv': _L1_xattn_in['Wv'], 'L1_xattn_bv': _L1_xattn_in['bv']}

def reference(x, ctx_2048, L0_xattn_theta_w, L0_xattn_theta_b, L0_xattn_phi_w, L0_xattn_phi_b, L0_xattn_g_w, L0_xattn_g_b, L0_xattn_w_w, L0_xattn_w_b, L0_xattn_bn_gamma, L0_xattn_bn_beta, L0_xattn_bn_mean, L0_xattn_bn_var, L1_xattn_Wq, L1_xattn_bq, L1_xattn_Wk, L1_xattn_bk, L1_xattn_Wv, L1_xattn_bv):
    import jax
    import jax.numpy as jnp

    def _L0_xattn_ref(x, x_2, theta_w, theta_b, phi_w, phi_b, g_w, g_b, w_w, w_b, bn_gamma, bn_beta, bn_mean, bn_var):
        import jax, jax.numpy as jnp
        import numpy as np
        B, C, CI, N = (16, 256, 128, 512)
        EPS = 1e-05

        def _conv1x1(w, b, x):
            return jnp.einsum('oc,bcn->bon', w, x) + b[None, :, None]
        g_x = _conv1x1(g_w, g_b, x_2).transpose(0, 2, 1)
        theta_x = _conv1x1(theta_w, theta_b, x).transpose(0, 2, 1)
        phi_x = _conv1x1(phi_w, phi_b, x_2)
        W = jnp.einsum('bnc,bcm->bnm', theta_x, phi_x) / phi_x.shape[-1]
        y = jnp.einsum('bnm,bmc->bnc', W, g_x).transpose(0, 2, 1)
        wy = _conv1x1(w_w, w_b, y)
        inv_std = jax.lax.rsqrt(bn_var + EPS)
        wy = bn_gamma[None, :, None] * (wy - bn_mean[None, :, None]) * inv_std[None, :, None] + bn_beta[None, :, None]
        return wy + x

    def _L1_xattn_ref(x1, x2, Wq, bq, Wk, bk, Wv, bv):
        import jax, jax.numpy as jnp
        import numpy as np
        B, C1, C2, N = (8, 256, 256, 512)
        D = C2 // 8
        q = jnp.einsum('bcn,dc->bnd', x1, Wq) + bq
        k = jnp.einsum('bcn,dc->bdn', x2, Wk) + bk[:, None]
        v = jnp.einsum('bcn,dc->bdn', x2, Wv) + bv[:, None]
        attn = jax.nn.softmax(jnp.einsum('bnd,bdm->bnm', q, k), axis=2)
        attn_out = jnp.einsum('bcm,bnm->bcn', v, attn)
        return attn_out + x1
    x = _L0_xattn_ref(x, ctx_2048, L0_xattn_theta_w, L0_xattn_theta_b, L0_xattn_phi_w, L0_xattn_phi_b, L0_xattn_g_w, L0_xattn_g_b, L0_xattn_w_w, L0_xattn_w_b, L0_xattn_bn_gamma, L0_xattn_bn_beta, L0_xattn_bn_mean, L0_xattn_bn_var)
    x = _L1_xattn_ref(x, ctx_2048, L1_xattn_Wq, L1_xattn_bq, L1_xattn_Wk, L1_xattn_bk, L1_xattn_Wv, L1_xattn_bv)
    return x

_drawn_inputs = setup_inputs


def setup_inputs(seed=0):
    import zlib

    import numpy as np

    out = dict(_drawn_inputs(seed))
    spreads = {}
    factors = {'L0_xattn_theta_w': 3.266,
     'L0_xattn_theta_b': 8.0,
     'L0_xattn_phi_w': 3.147,
     'L0_xattn_phi_b': 8.0,
     'L0_xattn_g_w': 3.456,
     'L0_xattn_g_b': 8.0,
     'L0_xattn_w_w': 3.179,
     'L0_xattn_w_b': 4.075,
     'L1_xattn_bk': 64.0,
     'L1_xattn_bv': 2.824,
     'L1_xattn_bq': 7.213}
    for name, (base, spread) in spreads.items():
        noise = np.random.default_rng([zlib.crc32(name.encode()), seed]).standard_normal(out[name].shape)
        drawn = base * np.exp(spread * noise) if base else spread * noise
        out[name] = jnp.asarray(drawn.astype(out[name].dtype))
    for name, factor in factors.items():
        out[name] = (out[name] * factor).astype(out[name].dtype)
    return out
```

```python
from collections import namedtuple
from contextlib import ExitStack

import concourse.bass as bass
from concourse import mybir

P = 128
F32 = mybir.dt.float32
F32R = mybir.dt.float32r
ALU = mybir.AluOpType
ACT = mybir.ActivationFunctionType
AX_X = mybir.AxisListType.X
EPS = 1e-5

COL_THETA_B, COL_BQ, COL_BK, COL_BV, COL_WB, COL_GAMMA, COL_BETA, COL_MEAN, COL_VAR = 0, 1, 2, 3, 5, 7, 9, 11, 13
COLS = 15


class Batch(namedtuple("Batch", "pair parity")):

    def number(self):
        return self.pair * 2 + self.parity

    def plus(self, n):
        both = self.parity + n
        return Batch(self.pair + both // 2, both % 2)


def count(batch, per_batch, done):
    return batch.number() * per_batch + done


def xattn_kernel(nc, x, ctx, w_pgv, w_pack_a, w_pack_b, CI, D, out):
    B, C, N = x.shape
    A_COLS, B_COLS = w_pack_a.shape[1], w_pack_b.shape[1]
    CK, NT, REP = C // P, N // P, P // D
    PG = 2 * CI
    assert CI == P and N == 512 and PG + C == 512 and REP == NT and B % 2 == 0

    x_rows = x.rearrange("b (k p) n -> b p k n", p=P)
    ctx_rows = ctx.rearrange("b (k p) n -> b p k n", p=P)
    out_rows = out.rearrange("b (k p) n -> b k p n", p=P)

    with ExitStack() as stack:
        def sb(name, shape, dt=F32):
            return stack.enter_context(nc.sbuf_tensor(name, shape, dt))

        def ps(name):
            return stack.enter_context(nc.psum_tensor(name, [P, 512], F32))

        def sem(name):
            return stack.enter_context(nc.semaphore(name))

        s_ps = [ps(f"s_ps{j}") for j in range(NT)]
        pv_ps = [ps(f"pv_ps{c}") for c in range(CK)]
        ring_ps = [ps(f"ring_ps{r}") for r in range(2)]
        k_ps = pv_ps[0]
        q_ps, q_st_ps = s_ps[2], s_ps[3]
        RING = ["pgv0", "pgv1", "pgv2", "pgv3", "theta", "mt", "t1", "wy0", "wy1"]

        def bank(batch, item):
            return ring_ps[(batch.parity * len(RING) + RING.index(item)) % 2]

        def pt_bank(i, last_batch):
            return [ring_ps[0], ring_ps[1], s_ps[0], s_ps[1]][i] if last_batch else s_ps[i]

        pack_a = sb("pack_a", [P, A_COLS])
        pack_b = sb("pack_b", [P, B_COLS])

        def views(pack, widths):
            ends = [sum(widths[:n + 1]) for n in range(len(widths))]
            return [pack[:, end - width:end] for end, width in zip(ends, widths)]

        wk, bpg, ident, vec = views(pack_a, (CK * D, PG, P, COLS))
        wtheta_raw, ww_raw, wq = views(pack_b, (CK * CI, CK * CI, CK * D))
        wk, wq, wtheta_raw, ww_raw = (w.rearrange("p (k n) -> p k n", k=CK) for w in (wk, wq, wtheta_raw, ww_raw))
        pgv_raw = sb("pgv_raw", [P, CK, 512])
        pgv_wh = sb("pgv_wh", [P, CK, 512], F32R)
        pgv_wl = sb("pgv_wl", [P, CK, 512], F32R)
        wtheta_h = sb("wtheta_h", [P, CK, CI], F32R)
        wtheta_l = sb("wtheta_l", [P, CK, CI], F32R)
        ww_scaled = sb("ww_scaled", [P, CK, CI])
        ww = sb("ww", [P, C])
        stack_sel = {(w, part): sb(f"sel_{w}_{part}", [P, NT, REP, D], F32R) for w in "qk" for part in "hl"}
        STACK_GROUPS = {("q", "h"): (0, 1), ("q", "l"): (2, 3), ("k", "h"): (0, 2), ("k", "l"): (1, 3)}
        bn = sb("bn", [P, 8, CK])
        bn_shift = sb("bn_shift", [P, CK])
        x_sb = [sb(f"x_sb{p}", [P, CK, N]) for p in range(2)]
        ctx_sb = [sb(f"ctx_sb{p}", [P, CK, N]) for p in range(2)]
        ctx_h = [sb(f"ctx_h{p}", [P, CK, N], F32R) for p in range(2)]
        ctx_l = [sb(f"ctx_l{p}", [P, CK, N], F32R) for p in range(2)]
        x_h = sb("x_h", [P, CK, N], F32R)
        x_l = sb("x_l", [P, CK, N], F32R)
        phig = sb("phig", [P, NT, PG])
        theta_h = sb("theta_h", [P, N], F32R)
        theta_l = sb("theta_l", [P, N], F32R)
        mt = sb("mt", [P, CI])
        t1_h = sb("t1_h", [P, C], F32R)
        t1_l = sb("t1_l", [P, C], F32R)
        x1 = [sb(f"x1_{p}", [P, CK, N]) for p in range(2)]
        v_h = [sb(f"v_h{p}", [P, NT, C], F32R) for p in range(2)]
        v_l = [sb(f"v_l{p}", [P, NT, C], F32R) for p in range(2)]
        k_h, k_l = sb("k_h", [P, P], F32R), sb("k_l", [P, P], F32R)
        q_h, q_l = sb("q_h", [P, P], F32R), sb("q_l", [P, P], F32R)
        k_st, q_st = sb("k_st", [P, N], F32R), sb("q_st", [P, N], F32R)
        negmax = sb("negmax", [P, NT])
        rowsum = sb("rowsum", [P, NT])
        rowinv = sb("rowinv", [P, NT])
        probs = sb("probs", [P, NT, N])
        pt_h = sb("pt_h", [P, NT, N], F32R)
        pt_l = sb("pt_l", [P, NT, N], F32R)
        out_sb = [sb(f"out_sb{p}", [P, CK, N]) for p in range(2)]

        pack_a_loaded, pack_b_loaded = sem("pack_a_loaded"), sem("pack_b_loaded")
        pgv_loaded = sem("pgv_loaded")
        ctx_loaded = [sem(f"ctx_loaded{p}") for p in range(2)]
        x_loaded = [sem(f"x_loaded{p}") for p in range(2)]
        stored = [sem(f"stored{p}") for p in range(2)]
        bn_steps, std_ready = sem("bn_steps"), sem("std_ready")
        ww_scaled_done, ww_ready, ww_saved = sem("ww_scaled_done"), sem("ww_ready"), sem("ww_saved")
        weights_split, sel_steps = sem("weights_split"), sem("sel_steps")
        SEL_STEPS = 3 * len(stack_sel)
        ctx_h_done, ctx_l_done = sem("ctx_h_done"), sem("ctx_l_done")
        x_h_done, x_l_done = sem("x_h_done"), sem("x_l_done")
        k_ready, pgv_ready, theta_ready, mt_ready = sem("k_ready"), sem("pgv_ready"), sem("theta_ready"), sem("mt_ready")
        t1_ready, wy_ready, q_ready = sem("t1_ready"), sem("wy_ready"), sem("q_ready")
        k_st_ready, q_st_ready = sem("k_st_ready"), sem("q_st_ready")
        s_ready, pt_ready, pv_ready = sem("s_ready"), sem("pt_ready"), sem("pv_ready")
        kh_saved, vh_saved, thetah_saved, mt_saved = sem("kh_saved"), sem("vh_saved"), sem("thetah_saved"), sem("mt_saved")
        t1h_saved, qh_saved, exp_done, probs_done_act = sem("t1h_saved"), sem("qh_saved"), sem("exp_done"), sem("probs_done_act")
        k_st_saved, q_st_saved = sem("k_st_saved"), sem("q_st_saved")
        pth_saved = sem("pth_saved")
        pgv_saved, x1_saved, negmax_done, rowinv_done = sem("pgv_saved"), sem("x1_saved"), sem("negmax_done"), sem("rowinv_done")
        ptl_saved, out_saved, probs_done_dve = sem("ptl_saved"), sem("out_saved"), sem("probs_done_dve")
        kl_saved, ql_saved, thetal_saved, t1l_saved = sem("kl_saved"), sem("ql_saved"), sem("thetal_saved"), sem("t1l_saved")

        block = stack.enter_context(nc.Block())

        def run_slots(eng, slot):
            slot(Batch(-1, 1), True, False)
            slot(Batch(0, 0), True, True)
            slot(Batch(0, 1), True, True)
            with eng.Fori(1, B // 2 - 1) as pair:
                slot(Batch(pair, 0), True, True)
                slot(Batch(pair, 1), True, True)
            slot(Batch(B // 2 - 1, 0), True, True)
            slot(Batch(B // 2 - 1, 1), False, True)

        def is_at_least(batch, n):
            return batch.number() >= n if isinstance(batch.pair, int) else True

        def is_at_most(batch, n):
            return batch.number() <= n if isinstance(batch.pair, int) else n >= B - 3

        @block.sync
        def _(sp):
            sp.dma_start(ctx_sb[0][:], ctx_rows[0]).then_inc(ctx_loaded[0], 16)
            sp.dma_start(pack_a[:], w_pack_a).then_inc(pack_a_loaded, 16)
            sp.dma_start(x_sb[0][:], x_rows[0]).then_inc(x_loaded[0], 16)
            sp.dma_start(ctx_sb[1][:], ctx_rows[1]).then_inc(ctx_loaded[1], 16)
            sp.dma_start(x_sb[1][:], x_rows[1]).then_inc(x_loaded[1], 16)

            def slot(b, layer0, layer1):
                if not layer1:
                    return
                n, p = b.number(), b.parity
                if is_at_most(b, B - 3):
                    sp.wait_ge(ctx_h_done, count(b, 1, 1))
                    sp.wait_ge(ctx_l_done, count(b, 1, 1))
                    sp.wait_ge(k_ready, count(b, 1, 1))
                    sp.dma_start(ctx_sb[p][:], ctx_rows[n + 2]).then_inc(ctx_loaded[p], 16)
                    sp.wait_ge(x1_saved, count(b, CK, CK))
                    sp.dma_start(x_sb[p][:], x_rows[n + 2]).then_inc(x_loaded[p], 16)
                for c in range(CK):
                    sp.wait_ge(out_saved, count(b, CK, c + 1))
                    sp.dma_start(out_rows[n, c], out_sb[p][:, c, :]).then_inc(stored[p], 16)

            run_slots(sp, slot)
            for p in range(2):
                sp.wait_ge(stored[p], 16 * CK * (B // 2))

        @block.gpsimd
        def _(pool):
            def split_low(b):
                pool.wait_ge(ctx_h_done, count(b, 1, 1))
                nc.gpsimd.tensor_tensor(ctx_l[b.parity][:], ctx_sb[b.parity][:], ctx_h[b.parity][:].bitcast(F32),
                                        ALU.subtract).then_inc(ctx_l_done, 1)

            def split_x(a):
                pool.wait_ge(x_h_done, count(a, 1, 1))
                nc.gpsimd.tensor_tensor(x_l[:], x_sb[a.parity][:], x_h[:].bitcast(F32), ALU.subtract).then_inc(x_l_done, 1)

            for sel in stack_sel.values():
                nc.gpsimd.memset(sel[:].bitcast(mybir.dt.uint32), 0).then_inc(sel_steps, 1)
            pool.wait_ge(sel_steps, len(stack_sel))
            pool.wait_ge(pack_a_loaded, 16)
            for key, groups in STACK_GROUPS.items():
                for g in groups:
                    nc.gpsimd.tensor_copy(stack_sel[key][:, :, g, :],
                                          ident.rearrange("p (j d) -> p j d", j=NT)).then_inc(sel_steps, 1)
            split_x(Batch(0, 0))

            def slot(b, layer0, layer1):
                if is_at_most(b, B - 3):
                    split_low(b.plus(2))
                    split_x(b.plus(2))

            run_slots(pool, slot)

        @block.scalar
        def _(act):
            act.dma_start(pgv_raw[:], w_pgv.rearrange("(k p) n -> p k n", p=P)).then_inc(pgv_loaded, 16)
            act.dma_start(pack_b[:], w_pack_b).then_inc(pack_b_loaded, 16)
            act.wait_ge(ctx_loaded[0], 16)
            nc.scalar.copy(ctx_h[0][:], ctx_sb[0][:]).then_inc(ctx_h_done, 1)
            act.wait_ge(pack_a_loaded, 16)
            act.wait_ge(bn_steps, 1)
            nc.scalar.activation(bn[:, 1, :], bn[:, 0, :], ACT.Sqrt).then_inc(std_ready, 1)

            def save_stack(ready, a, src, dst, saved):
                act.wait_ge(ready, count(a, 1, 1))
                nc.scalar.copy(dst[:], src[:]).then_inc(saved, 1)

            def save_k_high(a):
                act.wait_ge(k_ready, count(a, 1, 1))
                nc.scalar.activation(k_h[:], k_ps[:, 0:P], ACT.Identity,
                                     bias=vec[:, COL_BK:COL_BK + 1]).then_inc(kh_saved, 1)

            def save_v_high(a, j):
                act.wait_ge(pgv_ready, count(a, NT, j + 1))
                nc.scalar.copy(v_h[a.parity][:, j, :], bank(a, f"pgv{j}")[:, PG:]).then_inc(vh_saved, 1)

            def exponential(b, j):
                act.wait_ge(negmax_done, count(b, NT, j + 1))
                nc.scalar.activation(probs[:, j, :], s_ps[j][:], ACT.Exp, bias=negmax[:, j:j + 1],
                                     accum_out=rowsum[:, j:j + 1]).then_inc(exp_done, 1)

            def normalise(b, j):
                act.wait_ge(rowinv_done, count(b, 2, 2))
                nc.scalar.activation(probs[:, j, :], probs[:, j, :], ACT.Copy,
                                     scale=rowinv[:, j:j + 1]).then_inc(probs_done_act, 1)

            def slot(b, layer0, layer1):
                a = b.plus(1)
                if layer0:
                    save_k_high(a)
                if layer1:
                    exponential(b, 0)
                    exponential(b, 1)
                if layer0:
                    save_v_high(a, 0)
                if layer1:
                    exponential(b, 2)
                    exponential(b, 3)
                if layer0:
                    save_v_high(a, 1)
                    save_stack(k_st_ready, a, k_ps, k_st, k_st_saved)
                if layer1 and layer0:
                    normalise(b, 2)
                if layer0:
                    save_v_high(a, 2)
                if layer0:
                    save_v_high(a, 3)
                if layer1 and layer0:
                    normalise(b, 3)
                if layer0:
                    act.wait_ge(theta_ready, count(a, 1, 1))
                    nc.scalar.activation(theta_h[:], bank(a, "theta")[:], ACT.Identity,
                                         bias=vec[:, COL_THETA_B:COL_THETA_B + 1]).then_inc(thetah_saved, 1)
                if layer1:
                    for i in range(NT):
                        act.wait_ge(pt_ready, count(b, NT, i + 1))
                        nc.scalar.copy(pt_h[:, i, :], pt_bank(i, not layer0)[:]).then_inc(pth_saved, 1)
                if layer0:
                    act.wait_ge(mt_ready, count(a, 1, 1))
                    nc.scalar.copy(mt[:], bank(a, "mt")[:, 0:CI]).then_inc(mt_saved, 1)
                    act.wait_ge(t1_ready, count(a, 1, 1))
                    nc.scalar.copy(t1_h[:], bank(a, "t1")[:, 0:C]).then_inc(t1h_saved, 1)
                    act.wait_ge(q_ready, count(a, 1, 1))
                    nc.scalar.activation(q_h[:], q_ps[:, 0:P], ACT.Identity,
                                         bias=vec[:, COL_BQ:COL_BQ + 1]).then_inc(qh_saved, 1)
                    save_stack(q_st_ready, a, q_st_ps, q_st, q_st_saved)

            run_slots(act, slot)

        @block.vector
        def _(dve):
            def split_high(b):
                dve.wait_ge(ctx_loaded[b.parity], (b.pair + 1) * 16)
                nc.vector.tensor_copy(ctx_h[b.parity][:], ctx_sb[b.parity][:]).then_inc(ctx_h_done, 1)

            def split_x_high(a):
                dve.wait_ge(x_loaded[a.parity], (a.pair + 1) * 16)
                if is_at_least(a, 1):
                    dve.wait_ge(theta_ready, count(a.plus(-1), 1, 1))
                nc.vector.tensor_copy(x_h[:], x_sb[a.parity][:]).then_inc(x_h_done, 1)

            steps = [0]
            var, std, inv, sq, half, scale, diff, prod = (bn[:, k, :] for k in range(8))

            def step(instruction):
                steps[0] += 1
                instruction.then_inc(bn_steps, 1)
                dve.wait_ge(bn_steps, steps[0])

            def col(c):
                return vec[:, c:c + CK]

            dve.wait_ge(ctx_h_done, 1)
            nc.vector.tensor_tensor(ctx_l[0][:], ctx_sb[0][:], ctx_h[0][:].bitcast(F32), ALU.subtract).then_inc(ctx_l_done, 1)
            dve.wait_ge(pack_a_loaded, 16)
            step(nc.vector.tensor_scalar(var, col(COL_VAR), EPS, None, ALU.add))

            dve.wait_ge(pgv_loaded, 16)
            nc.vector.tensor_copy(pgv_wh[:], pgv_raw[:]).then_inc(weights_split, 1)
            dve.wait_ge(weights_split, 1)
            nc.vector.tensor_tensor(pgv_wl[:], pgv_raw[:], pgv_wh[:].bitcast(F32), ALU.subtract).then_inc(weights_split, 1)
            split_x_high(Batch(0, 0))
            dve.wait_ge(pack_b_loaded, 16)
            nc.vector.tensor_copy(wtheta_h[:], wtheta_raw).then_inc(weights_split, 1)
            dve.wait_ge(weights_split, 3)
            nc.vector.tensor_tensor(wtheta_l[:], wtheta_raw, wtheta_h[:].bitcast(F32), ALU.subtract).then_inc(weights_split, 1)

            def batch_norm():
                dve.wait_ge(std_ready, 1)
                step(nc.vector.reciprocal(inv, std))
                step(nc.vector.tensor_tensor(sq, inv, inv, ALU.mult))
                step(nc.vector.tensor_tensor(half, sq, var, ALU.mult))
                step(nc.vector.tensor_scalar(half, half, -0.5, 1.5, ALU.mult, ALU.add))
                step(nc.vector.tensor_tensor(inv, inv, half, ALU.mult))
                step(nc.vector.tensor_tensor(scale, inv, col(COL_GAMMA), ALU.mult))
                for c in range(CK):
                    nc.vector.tensor_scalar(ww_scaled[:, c, :], ww_raw[:, c, :], scale[:, c:c + 1], 1.0 / N,
                                            ALU.mult, ALU.mult).then_inc(ww_scaled_done, 1)
                step(nc.vector.tensor_tensor(diff, col(COL_WB), col(COL_MEAN), ALU.subtract))
                step(nc.vector.tensor_tensor(prod, diff, scale, ALU.mult))
                step(nc.vector.tensor_tensor(bn_shift[:], prod, col(COL_BETA), ALU.add))

            def save_ww():
                dve.wait_ge(ww_ready, 1)
                nc.vector.tensor_copy(ww[:], s_ps[1][:, 0:C]).then_inc(ww_saved, 1)

            def row_max(b, j):
                dve.wait_ge(s_ready, count(b, NT, j + 1))
                nc.vector.tensor_reduce(negmax[:, j:j + 1], s_ps[j][:], AX_X, ALU.max, negate=True).then_inc(negmax_done, 1)

            def row_inverse(b, h):
                dve.wait_ge(exp_done, count(b, NT, 2 * h + 2))
                nc.vector.reciprocal(rowinv[:, 2 * h:2 * h + 2], rowsum[:, 2 * h:2 * h + 2]).then_inc(rowinv_done, 1)

            def normalise(b, j):
                dve.wait_ge(rowinv_done, count(b, 2, j // 2 + 1))
                nc.vector.tensor_scalar(probs[:, j, :], probs[:, j, :], rowinv[:, j:j + 1], None,
                                        ALU.mult).then_inc(probs_done_dve, 1)

            def save_pgv(a, j):
                src = bank(a, f"pgv{j}")
                dve.wait_ge(vh_saved, count(a, NT, j + 1))
                nc.vector.tensor_tensor(phig[:, j, :], src[:, 0:PG], bpg, ALU.add)
                nc.vector.tensor_tensor(v_l[a.parity][:, j, :], src[:, PG:], v_h[a.parity][:, j, :].bitcast(F32),
                                        ALU.subtract).then_inc(pgv_saved, 1)

            def save_low(high_saved, a, src, bias, high, low, saved):
                dve.wait_ge(high_saved, count(a, 1, 1))
                if bias is None:
                    nc.vector.tensor_tensor(low[:], src, high[:].bitcast(F32), ALU.subtract).then_inc(saved, 1)
                else:
                    nc.vector.scalar_tensor_tensor(low[:], src, vec[:, bias:bias + 1], high[:].bitcast(F32),
                                                   ALU.add, ALU.subtract).then_inc(saved, 1)

            def save_x1(a, c):
                dve.wait_ge(wy_ready, count(a, CK, c + 1))
                if c == 0:
                    dve.wait_ge(x_loaded[a.parity], (a.pair + 1) * 16)
                nc.vector.scalar_tensor_tensor(x1[a.parity][:, c, :], bank(a, f"wy{c}")[:], bn_shift[:, c:c + 1],
                                               x_sb[a.parity][:, c, :], ALU.add, ALU.add).then_inc(x1_saved, 1)

            def save_out(b, c):
                dve.wait_ge(pv_ready, count(b, CK, c + 1))
                if c == 0 and is_at_least(b, 2):
                    dve.wait_ge(stored[b.parity], b.pair * (16 * CK))
                nc.vector.scalar_tensor_tensor(out_sb[b.parity][:, c, :], pv_ps[c][:], vec[:, COL_BV + c:COL_BV + c + 1],
                                               x1[b.parity][:, c, :], ALU.add, ALU.add).then_inc(out_saved, 1)

            def save_pt_low(b, last_batch):
                for i in range(NT):
                    dve.wait_ge(pth_saved, count(b, NT, i + 1))
                    nc.vector.tensor_tensor(pt_l[:, i, :], pt_bank(i, last_batch)[:], pt_h[:, i, :].bitcast(F32),
                                            ALU.subtract).then_inc(ptl_saved, 1)

            def slot(b, layer0, layer1):
                a = b.plus(1)
                if layer1:
                    row_max(b, 0)
                if layer0:
                    save_low(kh_saved, a, k_ps[:, 0:P], COL_BK, k_h, k_l, kl_saved)
                if layer1:
                    for j in range(1, NT):
                        row_max(b, j)
                else:
                    batch_norm()
                if layer0:
                    save_pgv(a, 0)
                else:
                    save_out(b.plus(-1), 1)
                if layer1:
                    row_inverse(b, 0)
                    if not layer0:
                        normalise(b, 0)
                        normalise(b, 1)
                    row_inverse(b, 1)
                    if layer0:
                        normalise(b, 0)
                    else:
                        normalise(b, 2)
                        normalise(b, 3)
                if layer0:
                    save_pgv(a, 1)
                    if layer1:
                        normalise(b, 1)
                    save_pgv(a, 2)
                    save_pgv(a, 3)
                if not layer1:
                    save_ww()
                if is_at_most(b, B - 3):
                    split_high(b.plus(2))
                if layer0:
                    save_low(thetah_saved, a, bank(a, "theta")[:], COL_THETA_B, theta_h, theta_l, thetal_saved)
                if layer1:
                    save_pt_low(b, not layer0)
                if layer0:
                    save_low(t1h_saved, a, bank(a, "t1")[:, 0:C], None, t1_h, t1_l, t1l_saved)
                if is_at_most(b, B - 3):
                    split_x_high(b.plus(2))
                if layer0:
                    for c in range(CK):
                        save_x1(a, c)
                if layer1:
                    save_out(b, 0)
                if layer0:
                    save_low(qh_saved, a, q_ps[:, 0:P], COL_BQ, q_h, q_l, ql_saved)
                if layer1 and not is_at_most(b, B - 3) and layer0:
                    pass
                elif layer1:
                    save_out(b, 1)

            run_slots(dve, slot)

        @block.tensor
        def _(pe):
            pe.wait_ge(pack_a_loaded, 16)

            def transpose_ww():
                pe.wait_ge(ww_scaled_done, CK)
                for c in range(CK):
                    last = nc.tensor.transpose(s_ps[1][:, c * P:(c + 1) * P], ww_scaled[:, c, :], ident)
                last.then_inc(ww_ready, 1)

            def project_32(w, src, dst):
                for kk in range(CK):
                    for j in range(NT):
                        last = nc.tensor.matmul(dst[j * D:(j + 1) * D, 0:P], w[:, kk, :], src[:, kk, j * P:(j + 1) * P],
                                                start=(kk == 0), stop=(kk == CK - 1), tile_position=(0, j * D))
                return last

            def stack_parts(which, high, low, dst):
                for j in range(NT):
                    for part, src in (("h", high), ("l", low)):
                        last = nc.tensor.matmul(dst[:, j * P:(j + 1) * P],
                                                stack_sel[which, part][:, j].rearrange("p r d -> p (r d)"), src[:],
                                                start=(part == "h"), stop=(part == "l"))
                return last

            def split_product(dst, pairs):
                terms = [(s[i], m[j]) for i, j in ((0, 0), (0, 1), (1, 0)) for s, m in pairs]
                for n, (stationary, moving) in enumerate(terms):
                    last = nc.tensor.matmul(dst, stationary, moving, start=(n == 0), stop=(n == len(terms) - 1))
                return last

            def project_k(a):
                pe.wait_ge(ctx_loaded[a.parity], (a.pair + 1) * 16)
                if is_at_least(a, 2):
                    pe.wait_ge(out_saved, count(a.plus(-2), CK, 1))
                project_32(wk, ctx_sb[a.parity], k_ps).then_inc(k_ready, 1)

            def stack_k(a):
                pe.wait_ge(kl_saved, count(a, 1, 1))
                if is_at_most(a, 0):
                    pe.wait_ge(sel_steps, SEL_STEPS)
                stack_parts("k", k_h, k_l, k_ps).then_inc(k_st_ready, 1)

            def project_pgv(a, j):
                p = a.parity
                if j == 0:
                    pe.wait_ge(ctx_l_done, count(a, 1, 1))
                if j >= 2:
                    pe.wait_ge(pgv_saved, count(a, NT, j - 1))
                elif is_at_least(a, 1):
                    pe.wait_ge(x1_saved, count(a.plus(-1), CK, j + 1))
                if is_at_most(a, 0):
                    pe.wait_ge(weights_split, 2)
                split_product(bank(a, f"pgv{j}")[:],
                              [((ctx_h[p][:, kk, j * P:(j + 1) * P], ctx_l[p][:, kk, j * P:(j + 1) * P]),
                                (pgv_wh[:, kk, :], pgv_wl[:, kk, :])) for kk in range(CK)]).then_inc(pgv_ready, 1)

            def project_theta(a):
                pe.wait_ge(x_l_done, count(a, 1, 1))
                pe.wait_ge(pgv_saved, count(a, NT, 3))
                if is_at_most(a, 0):
                    pe.wait_ge(weights_split, 4)
                split_product(bank(a, "theta")[:],
                              [((wtheta_h[:, kk, :], wtheta_l[:, kk, :]), (x_h[:, kk, :], x_l[:, kk, :]))
                               for kk in range(CK)]).then_inc(theta_ready, 1)

            def product_mt(a):
                pe.wait_ge(pgv_saved, count(a, NT, NT))
                for j in range(NT):
                    last = nc.tensor.matmul(bank(a, "mt")[:, 0:CI], phig[:, j, CI:PG], phig[:, j, 0:CI],
                                            start=(j == 0), stop=(j == NT - 1))
                last.then_inc(mt_ready, 1)

            def product_t1(a):
                pe.wait_ge(thetal_saved, count(a, 1, 1))
                pe.wait_ge(mt_saved, count(a, 1, 1))
                if is_at_most(a, 0):
                    pe.wait_ge(ww_saved, 1)
                nc.tensor.matmul(bank(a, "t1")[:, 0:C], mt[:], ww[:], start=True, stop=True).then_inc(t1_ready, 1)

            def product_wy(a, c):
                if c == 0:
                    pe.wait_ge(t1l_saved, count(a, 1, 1))
                cols = slice(c * P, (c + 1) * P)
                split_product(bank(a, f"wy{c}")[:],
                              [((t1_h[:, cols], t1_l[:, cols]), (theta_h[:], theta_l[:]))]).then_inc(wy_ready, 1)

            def project_q(a):
                pe.wait_ge(x1_saved, count(a, CK, CK))
                if is_at_most(a, 0):
                    pe.wait_ge(pack_b_loaded, 16)
                if is_at_least(a, 1):
                    pe.wait_ge(ptl_saved, count(a.plus(-1), NT, NT))
                project_32(wq, x1[a.parity], q_ps).then_inc(q_ready, 1)

            def stack_q(a):
                pe.wait_ge(ql_saved, count(a, 1, 1))
                stack_parts("q", q_h, q_l, q_st_ps).then_inc(q_st_ready, 1)

            def scores(b):
                pe.wait_ge(q_st_saved, count(b, 1, 1))
                pe.wait_ge(k_st_saved, count(b, 1, 1))
                for j in range(NT):
                    nc.tensor.matmul(s_ps[j][:], q_st[:, j * P:(j + 1) * P], k_st[:], start=True,
                                     stop=True).then_inc(s_ready, 1)

            def transpose_probs(b, last_batch):
                def block(i, j):
                    return nc.tensor.transpose(pt_bank(i, last_batch)[:, j * P:(j + 1) * P], probs[:, j, i * P:(i + 1) * P], ident)

                if last_batch:
                    for j in range(NT):
                        pe.wait_ge(probs_done_dve, count(b, 2, j + 1))
                        for i in range(NT):
                            done = block(i, j)
                            if j == NT - 1:
                                done.then_inc(pt_ready, 1)
                else:
                    pe.wait_ge(probs_done_dve, count(b, 2, 2))
                    pe.wait_ge(probs_done_act, count(b, 2, 2))
                    for i in range(NT):
                        for j in range(NT):
                            done = block(i, j)
                        done.then_inc(pt_ready, 1)

            def attend(b, c, steps):
                p = b.parity
                for step in steps:
                    i, n = divmod(step, 3)
                    if step == 0:
                        if c == 0 and is_at_most(b, B - 2):
                            pe.wait_ge(k_st_saved, count(b.plus(1), 1, 1))
                        if is_at_least(b, 1):
                            pe.wait_ge(out_saved, count(b.plus(-1), CK, c + 1))
                    if c == 0 and n == 0:
                        pe.wait_ge(ptl_saved, count(b, NT, i + 1))
                    v, pt = ((v_h, pt_h), (v_h, pt_l), (v_l, pt_h))[n]
                    last = nc.tensor.matmul(pv_ps[c][:], v[p][:, i, c * P:(c + 1) * P], pt[:, i, :],
                                            start=(step == 0), stop=(step == 3 * NT - 1))
                if 3 * NT - 1 in steps:
                    last.then_inc(pv_ready, 1)

            def slot(b, layer0, layer1):
                a = b.plus(1)
                ahead = layer0 and is_at_least(b, 0) and not is_at_least(b, 1)
                if layer0 and not ahead:
                    project_k(a)
                if layer1:
                    scores(b)
                if layer0 and not ahead:
                    project_pgv(a, 0)
                if layer0:
                    project_pgv(a, 1)
                    stack_k(a)
                    project_pgv(a, 2)
                    project_pgv(a, 3)
                    project_theta(a)
                if layer1:
                    transpose_probs(b, not layer0)
                if not layer1:
                    transpose_ww()
                if layer0:
                    product_mt(a)
                if layer1:
                    attend(b, 0, range(0, 3))
                if layer0:
                    product_t1(a)
                if layer1:
                    attend(b, 0, range(3, 3 * NT))
                if layer0:
                    product_wy(a, 0)
                    product_wy(a, 1)
                if layer1:
                    attend(b, 1, range(0, 5))
                else:
                    project_k(a.plus(1))
                if layer0:
                    project_q(a)
                if layer1:
                    attend(b, 1, range(5, 9))
                else:
                    project_pgv(a.plus(1), 0)
                if layer0:
                    stack_q(a)
                if layer1:
                    attend(b, 1, range(9, 3 * NT))

            run_slots(pe, slot)


def pack_vectors(C, CI, D, theta_b, bq, bk, over_c):
    import numpy as np

    cols = [theta_b.reshape(CI, 1), np.concatenate([bq] * (P // D)).reshape(P, 1),
            np.concatenate([bk] * (P // D)).reshape(P, 1)]
    cols += [v.reshape(C // P, P).T for v in over_c]
    return np.ascontiguousarray(np.concatenate(cols, axis=1))


def kernel(**inputs):
    import numpy as np
    import concourse.bacc as bacc
    from concourse.bass_utils import run_bass_kernel_spmd

    a = {k: np.asarray(v) for k, v in inputs.items()}
    B, C, N = a["x"].shape
    CI, D = a["L0_xattn_theta_w"].shape[0], a["L1_xattn_Wq"].shape[0]
    def rows_of(w):
        return w.reshape(C // P, P, -1).transpose(1, 0, 2).reshape(P, -1)

    vectors = pack_vectors(C, CI, D, a["L0_xattn_theta_b"], a["L1_xattn_bq"], a["L1_xattn_bk"],
                           [a["L1_xattn_bv"], a["L0_xattn_w_b"], a["L0_xattn_bn_gamma"],
                            a["L0_xattn_bn_beta"], a["L0_xattn_bn_mean"], a["L0_xattn_bn_var"]])
    b_pg = np.concatenate([a["L0_xattn_phi_b"], a["L0_xattn_g_b"]])
    arrays = {
        "x_dram": a["x"],
        "ctx_dram": a["ctx_2048"],
        "w_pgv_dram": np.concatenate([a["L0_xattn_phi_w"].T, a["L0_xattn_g_w"].T, a["L1_xattn_Wv"].T], axis=1),
        "w_pack_a_dram": np.concatenate([rows_of(a["L1_xattn_Wk"].T), np.broadcast_to(b_pg, (P, 2 * CI)),
                                         np.eye(P, dtype=np.float32), vectors], axis=1),
        "w_pack_b_dram": np.concatenate([rows_of(a["L0_xattn_theta_w"].T), rows_of(a["L0_xattn_w_w"]),
                                         rows_of(a["L1_xattn_Wq"].T)], axis=1),
    }
    arrays = {k: np.ascontiguousarray(v) for k, v in arrays.items()}
    nc = bacc.Bacc("TRN2", target_bir_lowering=False, num_devices=1)
    args = [nc.dram_tensor(k, v.shape, mybir.dt.from_np(v.dtype), kind="ExternalInput").ap() for k, v in arrays.items()]
    out = nc.dram_tensor("out_dram", (B, C, N), F32, kind="ExternalOutput").ap()
    xattn_kernel(nc, *args, CI, D, out)
    r = run_bass_kernel_spmd(nc, [arrays], core_ids=[0])
    return r.results[0]["out_dram"]
```

```python
from collections import namedtuple
from contextlib import ExitStack

import concourse.bass as bass
from concourse import mybir

P = 128
F32 = mybir.dt.float32
F32R = mybir.dt.float32r
ALU = mybir.AluOpType
ACT = mybir.ActivationFunctionType
AX_X = mybir.AxisListType.X
EPS = 1e-5
WARM_UP, KEEP_WARM = 13, 8

COL_THETA_B, COL_BQ, COL_BK, COL_BV, COL_WB, COL_GAMMA, COL_BETA, COL_MEAN, COL_VAR = 0, 1, 2, 3, 5, 7, 9, 11, 13
COLS = 15


class Batch(namedtuple("Batch", "pair parity")):

    def number(self):
        return self.pair * 2 + self.parity

    def plus(self, n):
        both = self.parity + n
        return Batch(self.pair + both // 2, both % 2)


def count(batch, per_batch, done):
    return batch.number() * per_batch + done


def xattn_kernel(nc, x, ctx, vectors, w_pgv, w_pack_a, w_pack_b, CI, D, out):
    B, C, N = x.shape
    A_COLS, B_COLS = w_pack_a.shape[1], w_pack_b.shape[1]
    CK, NT, REP = C // P, N // P, P // D
    PG = 2 * CI
    assert CI == P and N == 512 and PG + C == 512 and REP == NT and B % 2 == 0

    x_rows = x.rearrange("b (k p) n -> b p k n", p=P)
    ctx_rows = ctx.rearrange("b (k p) n -> b p k n", p=P)
    out_rows = out.rearrange("b (k p) n -> b k p n", p=P)

    with ExitStack() as stack:
        def sb(name, shape, dt=F32):
            return stack.enter_context(nc.sbuf_tensor(name, shape, dt))

        def ps(name):
            return stack.enter_context(nc.psum_tensor(name, [P, 512], F32))

        def sem(name):
            return stack.enter_context(nc.semaphore(name))

        s_ps = [ps(f"s_ps{j}") for j in range(NT)]
        pv_ps = [ps(f"pv_ps{c}") for c in range(CK)]
        ring_ps = [ps(f"ring_ps{r}") for r in range(2)]
        k_ps = pv_ps[0]
        q_ps, q_st_ps = s_ps[2], s_ps[3]
        RING = ["pgv0", "pgv1", "pgv2", "pgv3", "theta", "mt", "t1", "wy0", "wy1"]

        def bank(batch, item):
            return ring_ps[(batch.parity * len(RING) + RING.index(item)) % 2]

        def pt_bank(i, last_batch):
            return [ring_ps[0], ring_ps[1], s_ps[0], s_ps[1]][i] if last_batch else s_ps[i]

        vec = sb("vec", [P, COLS])
        pack_a = sb("pack_a", [P, A_COLS])
        pack_b = sb("pack_b", [P, B_COLS])

        def views(pack, widths):
            ends = [sum(widths[:n + 1]) for n in range(len(widths))]
            return [pack[:, end - width:end] for end, width in zip(ends, widths)]

        wk, bpg, ident = views(pack_a, (CK * P, PG, P))
        wtheta_raw, ww_raw, wq = views(pack_b, (CK * CI, CK * CI, CK * D))
        wk_raw, wq, wtheta_raw, ww_raw = (w.rearrange("p (k n) -> p k n", k=CK) for w in (wk, wq, wtheta_raw, ww_raw))
        pgv_raw = sb("pgv_raw", [P, CK, 512])
        pgv_wh = sb("pgv_wh", [P, CK, 512], F32R)
        pgv_wl = sb("pgv_wl", [P, CK, 512], F32R)
        wk_h = sb("wk_h", [P, CK, P], F32R)
        wk_l = sb("wk_l", [P, CK, P], F32R)
        wtheta_h = sb("wtheta_h", [P, CK, CI], F32R)
        wtheta_l = sb("wtheta_l", [P, CK, CI], F32R)
        ww_scaled = sb("ww_scaled", [P, CK, CI])
        ww = sb("ww", [P, C])
        HALF = N // 2
        stack_sel = sb("stack_sel", [P, 2, REP, D], F32R)
        K_LOW = Q_LOW = slice(2 * D, 4 * D)
        bn = sb("bn", [P, 8, CK])
        bn_shift = sb("bn_shift", [P, CK])
        warm = sb("warm", [P, N], mybir.dt.bfloat16)
        exp_warm = sb("exp_warm", [P, CK])
        x_sb = [sb(f"x_sb{p}", [P, CK, N]) for p in range(2)]
        ctx_sb = [sb(f"ctx_sb{p}", [P, CK, N]) for p in range(2)]
        ctx_h = [sb(f"ctx_h{p}", [P, CK, N], F32R) for p in range(2)]
        ctx_l = [sb(f"ctx_l{p}", [P, CK, N], F32R) for p in range(2)]
        x_h = sb("x_h", [P, CK, N], F32R)
        x_l = sb("x_l", [P, CK, N], F32R)
        phig = sb("phig", [P, NT, PG])
        theta_h = sb("theta_h", [P, N], F32R)
        theta_l = sb("theta_l", [P, N], F32R)
        mt = sb("mt", [P, CI])
        t1_h = sb("t1_h", [P, C], F32R)
        t1_l = sb("t1_l", [P, C], F32R)
        x1 = [sb(f"x1_{p}", [P, CK, N]) for p in range(2)]
        v_h = [sb(f"v_h{p}", [P, NT, C], F32R) for p in range(2)]
        v_l = [sb(f"v_l{p}", [P, NT, C], F32R) for p in range(2)]
        q_parts = sb("q_parts", [P, HALF], F32R)
        k_st = [sb(f"k_st{p}", [P, N], F32R) for p in range(2)]
        q_st = sb("q_st", [P, N], F32R)
        negmax = sb("negmax", [P, NT])
        rowsum = sb("rowsum", [P, NT])
        rowinv = sb("rowinv", [P, NT])
        probs = sb("probs", [P, NT, N])
        pt_h = sb("pt_h", [P, NT, N], F32R)
        pt_l = sb("pt_l", [P, NT, N], F32R)
        out_sb = [sb(f"out_sb{p}", [P, CK, N]) for p in range(2)]

        vec_loaded, pack_a_loaded, pack_b_loaded = sem("vec_loaded"), sem("pack_a_loaded"), sem("pack_b_loaded")
        pgv_loaded = sem("pgv_loaded")
        ctx_loaded = [sem(f"ctx_loaded{p}") for p in range(2)]
        x_loaded = [sem(f"x_loaded{p}") for p in range(2)]
        stored = [sem(f"stored{p}") for p in range(2)]
        bn_steps, std_ready = sem("bn_steps"), sem("std_ready")
        ww_scaled_done, ww_ready, ww_saved = sem("ww_scaled_done"), sem("ww_ready"), sem("ww_saved")
        warm_filled, pgv_wh_done = sem("warm_filled"), sem("pgv_wh_done")
        weights_split, sel_steps = sem("weights_split"), sem("sel_steps")
        SEL_STEPS = REP
        ctx_l_part_done = sem("ctx_l_part_done")
        ctx_h_done, ctx_l_done = sem("ctx_h_done"), sem("ctx_l_done")
        x_h_done, x_l_done = sem("x_h_done"), sem("x_l_done")
        k_ready, pgv_ready, theta_ready, mt_ready = sem("k_ready"), sem("pgv_ready"), sem("theta_ready"), sem("mt_ready")
        t1_ready, wy_ready, q_ready = sem("t1_ready"), sem("wy_ready"), sem("q_ready")
        q_st_ready = sem("q_st_ready")
        s_ready, pt_ready, pv_ready = sem("s_ready"), sem("pt_ready"), sem("pv_ready")
        kh_saved, vh_saved, thetah_saved, mt_saved = sem("kh_saved"), sem("vh_saved"), sem("thetah_saved"), sem("mt_saved")
        t1h_saved, qh_saved, exp_done, probs_done_act = sem("t1h_saved"), sem("qh_saved"), sem("exp_done"), sem("probs_done_act")
        q_st_saved = sem("q_st_saved")
        pth_saved = sem("pth_saved")
        pgv_saved, x1_saved, negmax_done, rowinv_done = sem("pgv_saved"), sem("x1_saved"), sem("negmax_done"), sem("rowinv_done")
        ptl_saved, out_saved, probs_done_dve = sem("ptl_saved"), sem("out_saved"), sem("probs_done_dve")
        kl_saved, ql_saved, thetal_saved, t1l_saved = sem("kl_saved"), sem("ql_saved"), sem("thetal_saved"), sem("t1l_saved")

        block = stack.enter_context(nc.Block())

        def run_slots(eng, slot):
            slot(Batch(-1, 1), True, False)
            slot(Batch(0, 0), True, True)
            slot(Batch(0, 1), True, True)
            with eng.Fori(1, B // 2 - 1) as pair:
                slot(Batch(pair, 0), True, True)
                slot(Batch(pair, 1), True, True)
            slot(Batch(B // 2 - 1, 0), True, True)
            slot(Batch(B // 2 - 1, 1), False, True)

        def is_at_least(batch, n):
            return batch.number() >= n if isinstance(batch.pair, int) else True

        def is_at_most(batch, n):
            return batch.number() <= n if isinstance(batch.pair, int) else n >= B - 3

        def is_second(batch):
            return is_at_most(batch, 1) and is_at_least(batch, 1)

        def is_last_but_one(batch):
            return is_at_least(batch, B - 2) if isinstance(batch.pair, int) else False

        @block.sync
        def _(sp):
            sp.dma_start(ctx_sb[0][:], ctx_rows[0]).then_inc(ctx_loaded[0], 16)
            sp.dma_start(pgv_raw[:], w_pgv.rearrange("(k p) n -> p k n", p=P)).then_inc(pgv_loaded, 16)
            sp.dma_start(pack_a[:], w_pack_a).then_inc(pack_a_loaded, 16)
            sp.dma_start(x_sb[0][:], x_rows[0]).then_inc(x_loaded[0], 16)
            sp.dma_start(pack_b[:], w_pack_b).then_inc(pack_b_loaded, 16)
            sp.dma_start(ctx_sb[1][:], ctx_rows[1]).then_inc(ctx_loaded[1], 16)
            sp.dma_start(x_sb[1][:], x_rows[1]).then_inc(x_loaded[1], 16)

            def slot(b, layer0, layer1):
                if not layer1:
                    return
                n, p = b.number(), b.parity
                if is_at_most(b, B - 3):
                    sp.wait_ge(ctx_h_done, count(b, 1, 1))
                    sp.wait_ge(ctx_l_done, count(b, 1, 1))
                    if is_at_most(b, 0):
                        sp.wait_ge(ctx_l_part_done, 1)
                    sp.dma_start(ctx_sb[p][:], ctx_rows[n + 2]).then_inc(ctx_loaded[p], 16)
                    sp.wait_ge(x1_saved, count(b, CK, CK))
                    sp.dma_start(x_sb[p][:], x_rows[n + 2]).then_inc(x_loaded[p], 16)
                for c in range(CK):
                    sp.wait_ge(out_saved, count(b, CK, c + 1))
                    sp.dma_start(out_rows[n, c], out_sb[p][:, c, :]).then_inc(stored[p], 16)

            run_slots(sp, slot)
            for p in range(2):
                sp.wait_ge(stored[p], 16 * CK * (B // 2))

        @block.gpsimd
        def _(pool):
            def split_low(b):
                pool.wait_ge(ctx_h_done, count(b, 1, 1))
                nc.gpsimd.tensor_tensor(ctx_l[b.parity][:], ctx_sb[b.parity][:], ctx_h[b.parity][:].bitcast(F32),
                                        ALU.subtract).then_inc(ctx_l_done, 1)

            def split_x(a):
                pool.wait_ge(x_h_done, count(a, 1, 1))
                nc.gpsimd.tensor_tensor(x_l[:], x_sb[a.parity][:], x_h[:].bitcast(F32), ALU.subtract).then_inc(x_l_done, 1)

            pool.wait_ge(ctx_h_done, 1)
            nc.gpsimd.tensor_tensor(ctx_l[0][:, 1], ctx_sb[0][:, 1], ctx_h[0][:, 1].bitcast(F32),
                                    ALU.subtract).then_inc(ctx_l_part_done, 1)
            pool.wait_ge(pack_a_loaded, 16)
            by_part = ident.rearrange("p (l h d) -> p l h d", l=2, h=2)
            for g in range(REP):
                nc.gpsimd.tensor_copy(stack_sel[:, :, g, :], by_part[:, g % 2]).then_inc(sel_steps, 1)
            split_x(Batch(0, 0))

            def slot(b, layer0, layer1):
                if is_at_most(b, B - 3):
                    split_low(b.plus(2))
                    split_x(b.plus(2))

            run_slots(pool, slot)

        @block.scalar
        def _(act):
            act.dma_start(vec[:], vectors).then_inc(vec_loaded, 16)
            act.wait_ge(bn_steps, 1)
            nc.scalar.activation(bn[:, 1, :], bn[:, 0, :], ACT.Sqrt).then_inc(std_ready, 1)
            act.wait_ge(ctx_loaded[0], 16)
            nc.scalar.copy(ctx_h[0][:], ctx_sb[0][:]).then_inc(ctx_h_done, 1)
            act.wait_ge(pgv_loaded, 16)
            nc.scalar.copy(pgv_wh[:], pgv_raw[:]).then_inc(pgv_wh_done, 1)

            def save_k_high(a):
                act.wait_ge(k_ready, count(a, 1, 1))
                nc.scalar.activation(k_st[a.parity][:], k_ps[:], ACT.Identity,
                                     bias=vec[:, COL_BK:COL_BK + 1]).then_inc(kh_saved, 1)

            def save_v_high(a, j):
                act.wait_ge(pgv_ready, count(a, NT, j + 1))
                nc.scalar.copy(v_h[a.parity][:, j, :], bank(a, f"pgv{j}")[:, PG:]).then_inc(vh_saved, 1)

            def exponential(b, j):
                act.wait_ge(negmax_done, count(b, NT, j + 1))
                nc.scalar.activation(probs[:, j, :], s_ps[j][:], ACT.Exp, bias=negmax[:, j:j + 1],
                                     accum_out=rowsum[:, j:j + 1]).then_inc(exp_done, 1)

            def normalise(b, j):
                act.wait_ge(rowinv_done, count(b, 2, 2))
                nc.scalar.activation(probs[:, j, :], probs[:, j, :], ACT.Copy,
                                     scale=rowinv[:, j:j + 1]).then_inc(probs_done_act, 1)

            def save_pt_high(b, last_batch):
                for i in range(NT):
                    act.wait_ge(pt_ready, count(b, NT, i + 1))
                    nc.scalar.copy(pt_h[:, i, :], pt_bank(i, last_batch)[:]).then_inc(pth_saved, 1)

            def save_theta_high(a):
                act.wait_ge(theta_ready, count(a, 1, 1))
                nc.scalar.activation(theta_h[:], bank(a, "theta")[:], ACT.Identity,
                                     bias=vec[:, COL_THETA_B:COL_THETA_B + 1]).then_inc(thetah_saved, 1)

            def save_mt(a):
                act.wait_ge(mt_ready, count(a, 1, 1))
                nc.scalar.copy(mt[:], bank(a, "mt")[:, 0:CI]).then_inc(mt_saved, 1)

            def save_t1_high(a):
                act.wait_ge(t1_ready, count(a, 1, 1))
                nc.scalar.copy(t1_h[:], bank(a, "t1")[:, 0:C]).then_inc(t1h_saved, 1)

            def save_q_high(a):
                act.wait_ge(q_ready, count(a, 1, 1))
                nc.scalar.activation(q_parts[:], q_ps[:, 0:HALF], ACT.Identity,
                                     bias=vec[:, COL_BQ:COL_BQ + 1]).then_inc(qh_saved, 1)

            def save_q_stacked(a):
                act.wait_ge(q_st_ready, count(a, 1, 1))
                nc.scalar.copy(q_st[:], q_st_ps[:]).then_inc(q_st_saved, 1)

            def slot(b, layer0, layer1):
                a = b.plus(1)
                if not layer1:
                    for j in range(NT):
                        save_v_high(a, j)
                    save_theta_high(a)
                    save_mt(a)
                    save_t1_high(a)
                    save_k_high(a)
                    nc.scalar.activation(exp_warm[:], bn[:, 1, :], ACT.Exp)
                    save_q_high(a)
                    save_k_high(a.plus(1))
                    save_v_high(a.plus(1), 0)
                    save_q_stacked(a)
                    save_v_high(a.plus(1), 1)
                elif is_second(a):
                    exponential(b, 0)
                    save_v_high(a, 2)
                    exponential(b, 1)
                    save_v_high(a, 3)
                    exponential(b, 2)
                    exponential(b, 3)
                    normalise(b, 2)
                    normalise(b, 3)
                    save_theta_high(a)
                    save_mt(a)
                    save_pt_high(b, False)
                    save_t1_high(a)
                    save_q_high(a)
                    save_q_stacked(a)
                elif layer0:
                    exponential(b, 0)
                    save_v_high(a, 0)
                    exponential(b, 1)
                    exponential(b, 2)
                    save_v_high(a, 1)
                    exponential(b, 3)
                    normalise(b, 2)
                    normalise(b, 3)
                    save_v_high(a, 2)
                    save_k_high(a)
                    save_v_high(a, 3)
                    if is_last_but_one(b):
                        save_theta_high(a)
                        save_mt(a)
                        save_pt_high(b, False)
                    else:
                        save_pt_high(b, False)
                        save_theta_high(a)
                        save_mt(a)
                    save_t1_high(a)
                    save_q_high(a)
                    save_q_stacked(a)
                else:
                    for j in range(NT):
                        exponential(b, j)
                    save_pt_high(b, True)

            run_slots(act, slot)

        @block.vector
        def _(dve):
            def split_high(b):
                dve.wait_ge(ctx_loaded[b.parity], (b.pair + 1) * 16)
                nc.vector.tensor_copy(ctx_h[b.parity][:], ctx_sb[b.parity][:]).then_inc(ctx_h_done, 1)

            def split_x_high(a):
                dve.wait_ge(x_loaded[a.parity], (a.pair + 1) * 16)
                if is_at_least(a, 1):
                    dve.wait_ge(theta_ready, count(a.plus(-1), 1, 1))
                nc.vector.tensor_copy(x_h[:], x_sb[a.parity][:]).then_inc(x_h_done, 1)

            steps = [0]
            var, std, inv, sq, half, scale, diff, prod = (bn[:, k, :] for k in range(8))

            def step(instruction):
                steps[0] += 1
                instruction.then_inc(bn_steps, 1)
                dve.wait_ge(bn_steps, steps[0])

            def col(c):
                return vec[:, c:c + CK]

            def batch_norm_scale():
                dve.wait_ge(std_ready, 1)
                step(nc.vector.reciprocal(inv, std))
                step(nc.vector.tensor_tensor(sq, inv, inv, ALU.mult))
                step(nc.vector.tensor_tensor(half, sq, var, ALU.mult))
                step(nc.vector.tensor_scalar(half, half, -0.5, 1.5, ALU.mult, ALU.add))
                step(nc.vector.tensor_tensor(inv, inv, half, ALU.mult))
                step(nc.vector.tensor_tensor(scale, inv, col(COL_GAMMA), ALU.mult))

            def batch_norm_shift():
                step(nc.vector.tensor_tensor(diff, col(COL_WB), col(COL_MEAN), ALU.subtract))
                step(nc.vector.tensor_tensor(prod, diff, scale, ALU.mult))
                step(nc.vector.tensor_tensor(bn_shift[:], prod, col(COL_BETA), ALU.add))

            def scale_ww():
                dve.wait_ge(pack_b_loaded, 16)
                for c in range(CK):
                    nc.vector.tensor_scalar(ww_scaled[:, c, :], ww_raw[:, c, :], scale[:, c:c + 1], 1.0 / N,
                                            ALU.mult, ALU.mult).then_inc(ww_scaled_done, 1)

            nc.vector.memset(warm[:], 0.0).then_inc(warm_filled, 1)
            dve.wait_ge(vec_loaded, 16)
            step(nc.vector.tensor_scalar(var, col(COL_VAR), EPS, None, ALU.add))
            batch_norm_scale()
            dve.wait_ge(ctx_h_done, 1)
            nc.vector.tensor_tensor(ctx_l[0][:, 0], ctx_sb[0][:, 0], ctx_h[0][:, 0].bitcast(F32),
                                    ALU.subtract).then_inc(ctx_l_done, 1)
            dve.wait_ge(pgv_wh_done, 1)
            nc.vector.tensor_tensor(pgv_wl[:], pgv_raw[:], pgv_wh[:].bitcast(F32), ALU.subtract).then_inc(weights_split, 1)
            split_x_high(Batch(0, 0))

            def split_weights(raw, high, low, done):
                dve.wait_ge(pack_b_loaded, 16)
                nc.vector.tensor_copy(high[:], raw).then_inc(weights_split, 1)
                dve.wait_ge(weights_split, done + 1)
                nc.vector.tensor_tensor(low[:], raw, high[:].bitcast(F32), ALU.subtract).then_inc(weights_split, 1)

            def save_ww():
                dve.wait_ge(ww_ready, 1)
                nc.vector.tensor_copy(ww[:], s_ps[1][:, 0:C]).then_inc(ww_saved, 1)

            def row_max(b, j):
                dve.wait_ge(s_ready, count(b, NT, j + 1))
                nc.vector.tensor_reduce(negmax[:, j:j + 1], s_ps[j][:], AX_X, ALU.max, negate=True).then_inc(negmax_done, 1)

            def row_inverse(b, h):
                dve.wait_ge(exp_done, count(b, NT, 2 * h + 2))
                nc.vector.reciprocal(rowinv[:, 2 * h:2 * h + 2], rowsum[:, 2 * h:2 * h + 2]).then_inc(rowinv_done, 1)

            def normalise(b, j):
                dve.wait_ge(rowinv_done, count(b, 2, j // 2 + 1))
                nc.vector.tensor_scalar(probs[:, j, :], probs[:, j, :], rowinv[:, j:j + 1], None,
                                        ALU.mult).then_inc(probs_done_dve, 1)

            def save_pgv(a, j):
                src = bank(a, f"pgv{j}")
                dve.wait_ge(vh_saved, count(a, NT, j + 1))
                nc.vector.tensor_tensor(phig[:, j, :], src[:, 0:PG], bpg, ALU.add)
                nc.vector.tensor_tensor(v_l[a.parity][:, j, :], src[:, PG:], v_h[a.parity][:, j, :].bitcast(F32),
                                        ALU.subtract).then_inc(pgv_saved, 1)

            def save_k_low(a):
                dve.wait_ge(kh_saved, count(a, 1, 1))
                low = k_st[a.parity][K_LOW]
                nc.vector.scalar_tensor_tensor(low, k_ps[K_LOW], vec[K_LOW, COL_BK:COL_BK + 1], low.bitcast(F32),
                                               ALU.add, ALU.subtract).then_inc(kl_saved, 1)

            def save_q_low(a):
                dve.wait_ge(qh_saved, count(a, 1, 1))
                low = q_parts[Q_LOW]
                nc.vector.scalar_tensor_tensor(low, q_ps[Q_LOW, 0:HALF], vec[Q_LOW, COL_BQ:COL_BQ + 1], low.bitcast(F32),
                                               ALU.add, ALU.subtract).then_inc(ql_saved, 1)

            def save_low(high_saved, a, src, bias, high, low, saved):
                dve.wait_ge(high_saved, count(a, 1, 1))
                if bias is None:
                    nc.vector.tensor_tensor(low[:], src, high[:].bitcast(F32), ALU.subtract).then_inc(saved, 1)
                else:
                    nc.vector.scalar_tensor_tensor(low[:], src, vec[:, bias:bias + 1], high[:].bitcast(F32),
                                                   ALU.add, ALU.subtract).then_inc(saved, 1)

            def save_x1(a, c):
                dve.wait_ge(wy_ready, count(a, CK, c + 1))
                if c == 0:
                    dve.wait_ge(x_loaded[a.parity], (a.pair + 1) * 16)
                nc.vector.scalar_tensor_tensor(x1[a.parity][:, c, :], bank(a, f"wy{c}")[:], bn_shift[:, c:c + 1],
                                               x_sb[a.parity][:, c, :], ALU.add, ALU.add).then_inc(x1_saved, 1)

            def save_out(b, c):
                dve.wait_ge(pv_ready, count(b, CK, c + 1))
                if c == 0 and is_at_least(b, 2):
                    dve.wait_ge(stored[b.parity], b.pair * (16 * CK))
                nc.vector.scalar_tensor_tensor(out_sb[b.parity][:, c, :], pv_ps[c][:], vec[:, COL_BV + c:COL_BV + c + 1],
                                               x1[b.parity][:, c, :], ALU.add, ALU.add).then_inc(out_saved, 1)

            def save_pt_low(b, last_batch, tiles=range(NT)):
                for i in tiles:
                    dve.wait_ge(pth_saved, count(b, NT, i + 1))
                    nc.vector.tensor_tensor(pt_l[:, i, :], pt_bank(i, last_batch)[:], pt_h[:, i, :].bitcast(F32),
                                            ALU.subtract).then_inc(ptl_saved, 1)

            def save_t1_low(a):
                save_low(t1h_saved, a, bank(a, "t1")[:, 0:C], None, t1_h, t1_l, t1l_saved)

            def finish(a, b):
                if is_at_most(b, B - 3):
                    split_x_high(b.plus(2))
                for c in range(CK):
                    save_x1(a, c)
                if is_last_but_one(b):
                    save_q_low(a)
                    save_out(b, 0)
                else:
                    save_out(b, 0)
                    save_q_low(a)

            def save_theta_low(a):
                save_low(thetah_saved, a, bank(a, "theta")[:], COL_THETA_B, theta_h, theta_l, thetal_saved)

            def slot(b, layer0, layer1):
                a = b.plus(1)
                if not layer1:
                    dve.wait_ge(pack_a_loaded, 16)
                    save_pgv(a, 0)
                    split_weights(wtheta_raw, wtheta_h, wtheta_l, 1)
                    save_pgv(a, 1)
                    split_weights(wk_raw, wk_h, wk_l, 3)
                    save_pgv(a, 2)
                    scale_ww()
                    batch_norm_shift()
                    save_pgv(a, 3)
                    save_ww()
                    split_high(a.plus(1))
                    save_theta_low(a)
                    save_t1_low(a)
                    save_k_low(a)
                    split_x_high(a.plus(1))
                    for c in range(CK):
                        save_x1(a, c)
                    save_q_low(a)
                    save_k_low(a.plus(1))
                    save_pgv(a.plus(1), 0)
                    save_pgv(a.plus(1), 1)
                elif is_second(a):
                    row_max(b, 0)
                    row_max(b, 1)
                    row_max(b, 2)
                    save_pgv(a, 2)
                    row_max(b, 3)
                    save_pgv(a, 3)
                    row_inverse(b, 0)
                    row_inverse(b, 1)
                    normalise(b, 0)
                    normalise(b, 1)
                    save_theta_low(a)
                    split_high(b.plus(2))
                    save_pt_low(b, False)
                    save_t1_low(a)
                    finish(a, b)
                    save_out(b, 1)
                elif layer0:
                    for j in range(NT):
                        row_max(b, j)
                    save_pgv(a, 0)
                    row_inverse(b, 0)
                    save_pgv(a, 1)
                    row_inverse(b, 1)
                    normalise(b, 0)
                    normalise(b, 1)
                    save_pgv(a, 2)
                    save_k_low(a)
                    save_pgv(a, 3)
                    if is_last_but_one(b):
                        save_theta_low(a)
                        save_pt_low(b, False, range(3))
                        save_t1_low(a)
                        save_pt_low(b, False, range(3, NT))
                        finish(a, b)
                    else:
                        save_pt_low(b, False)
                        save_theta_low(a)
                        split_high(b.plus(2))
                        save_t1_low(a)
                        finish(a, b)
                        save_out(b, 1)
                else:
                    for j in range(NT):
                        row_max(b, j)
                    row_inverse(b, 0)
                    normalise(b, 0)
                    normalise(b, 1)
                    row_inverse(b, 1)
                    normalise(b, 2)
                    normalise(b, 3)
                    save_out(b.plus(-1), 1)
                    save_pt_low(b, True)
                    save_out(b, 0)
                    save_out(b, 1)

            run_slots(dve, slot)

        @block.tensor
        def _(pe):
            pe.wait_ge(warm_filled, 1)
            for _ in range(WARM_UP):
                nc.tensor.matmul(ring_ps[0][:], warm[:, 0:P], warm[:], start=True, stop=True)

            def transpose_ww():
                pe.wait_ge(pack_a_loaded, 16)
                pe.wait_ge(ww_scaled_done, CK)
                for c in range(CK):
                    last = nc.tensor.transpose(s_ps[1][:, c * P:(c + 1) * P], ww_scaled[:, c, :], ident)
                last.then_inc(ww_ready, 1)

            def split_product(dst, pairs, late_moving=True, middle=(), late=()):
                order = ((0, 0), (1, 0), (0, 1)) if late_moving else ((0, 0), (0, 1), (1, 0))
                for n, (i, j) in enumerate(order):
                    for sem_ready, value in ((), middle, late)[n]:
                        pe.wait_ge(sem_ready, value)
                    for m, (stationary, moving) in enumerate(pairs):
                        last = nc.tensor.matmul(dst, stationary[i], moving[j], start=(n == 0 and m == 0),
                                                stop=(n == 2 and m == len(pairs) - 1))
                return last

            def project_k(a):
                p = a.parity
                pe.wait_ge(ctx_l_done, count(a, 1, 1))
                if is_at_least(a, 2):
                    pe.wait_ge(out_saved, count(a.plus(-2), CK, 1))
                elif is_at_least(a, 1):
                    pe.wait_ge(kl_saved, count(a.plus(-1), 1, 1))
                if is_at_most(a, 0):
                    pe.wait_ge(weights_split, 5)
                split_product(k_ps[:], [((wk_h[:, kk, :], wk_l[:, kk, :]), (ctx_h[p][:, kk, :], ctx_l[p][:, kk, :]))
                                        for kk in range(CK)]).then_inc(k_ready, 1)

            def project_pgv(a, j):
                p = a.parity
                first = is_at_most(a, 0) and j == 0
                if j == 0 and not first:
                    pe.wait_ge(ctx_l_done, count(a, 1, 1))
                if j >= 2:
                    pe.wait_ge(pgv_saved, count(a, NT, j - 1))
                elif is_at_least(a, 1):
                    pe.wait_ge(x1_saved, count(a.plus(-1), CK, j + 1))
                if first:
                    pe.wait_ge(pgv_wh_done, 1)
                split_product(bank(a, f"pgv{j}")[:],
                              [((ctx_h[p][:, kk, j * P:(j + 1) * P], ctx_l[p][:, kk, j * P:(j + 1) * P]),
                                (pgv_wh[:, kk, :], pgv_wl[:, kk, :])) for kk in range(CK)],
                              middle=((ctx_l_part_done, 1), (ctx_l_done, 1)) if first else (),
                              late=((weights_split, 1),) if first else ()).then_inc(pgv_ready, 1)

            def project_theta(a):
                pe.wait_ge(x_l_done, count(a, 1, 1))
                pe.wait_ge(pgv_saved, count(a, NT, 3))
                if is_at_most(a, 0):
                    pe.wait_ge(weights_split, 3)
                split_product(bank(a, "theta")[:],
                              [((wtheta_h[:, kk, :], wtheta_l[:, kk, :]), (x_h[:, kk, :], x_l[:, kk, :]))
                               for kk in range(CK)]).then_inc(theta_ready, 1)

            def product_mt(a):
                pe.wait_ge(pgv_saved, count(a, NT, NT))
                for j in range(NT):
                    last = nc.tensor.matmul(bank(a, "mt")[:, 0:CI], phig[:, j, CI:PG], phig[:, j, 0:CI],
                                            start=(j == 0), stop=(j == NT - 1))
                last.then_inc(mt_ready, 1)

            def product_t1(a):
                pe.wait_ge(thetal_saved, count(a, 1, 1))
                pe.wait_ge(mt_saved, count(a, 1, 1))
                if is_at_most(a, 0):
                    pe.wait_ge(ww_saved, 1)
                nc.tensor.matmul(bank(a, "t1")[:, 0:C], mt[:], ww[:], start=True, stop=True).then_inc(t1_ready, 1)

            def product_wy(a, c):
                if c == 0:
                    pe.wait_ge(t1h_saved, count(a, 1, 1))
                cols = slice(c * P, (c + 1) * P)
                split_product(bank(a, f"wy{c}")[:],
                              [((t1_h[:, cols], t1_l[:, cols]), (theta_h[:], theta_l[:]))],
                              late_moving=False, late=((t1l_saved, count(a, 1, 1)),)).then_inc(wy_ready, 1)

            def project_q(a):
                pe.wait_ge(x1_saved, count(a, CK, CK))
                if is_at_most(a, 0):
                    pe.wait_ge(pack_b_loaded, 16)
                if is_at_least(a, 1):
                    pe.wait_ge(ptl_saved, count(a.plus(-1), NT, NT))
                for kk in range(CK):
                    for g in range(REP):
                        h = g % 2
                        last = nc.tensor.matmul(q_ps[g * D:(g + 1) * D, 0:HALF], wq[:, kk, :],
                                                x1[a.parity][:, kk, h * HALF:(h + 1) * HALF],
                                                start=(kk == 0), stop=(kk == CK - 1), tile_position=(0, g * D))
                last.then_inc(q_ready, 1)

            def stack_q(a):
                pe.wait_ge(ql_saved, count(a, 1, 1))
                if is_at_most(a, 0):
                    pe.wait_ge(sel_steps, SEL_STEPS)
                for h in range(2):
                    last = nc.tensor.matmul(q_st_ps[:, h * HALF:(h + 1) * HALF],
                                            stack_sel[:, h].rearrange("p r d -> p (r d)"), q_parts[:],
                                            start=True, stop=True)
                last.then_inc(q_st_ready, 1)

            def scores(b):
                pe.wait_ge(q_st_saved, count(b, 1, 1))
                pe.wait_ge(kl_saved, count(b, 1, 1))
                for j in range(NT):
                    nc.tensor.matmul(s_ps[j][:], q_st[:, j * P:(j + 1) * P], k_st[b.parity][:], start=True,
                                     stop=True).then_inc(s_ready, 1)

            def transpose_probs(b, last_batch):
                def block(i, j):
                    return nc.tensor.transpose(pt_bank(i, last_batch)[:, j * P:(j + 1) * P], probs[:, j, i * P:(i + 1) * P], ident)

                if last_batch:
                    for j in range(NT):
                        pe.wait_ge(probs_done_dve, count(b, 2, j + 1))
                        for i in range(NT):
                            done = block(i, j)
                            if j == NT - 1:
                                done.then_inc(pt_ready, 1)
                else:
                    pe.wait_ge(probs_done_dve, count(b, 2, 2))
                    pe.wait_ge(probs_done_act, count(b, 2, 2))
                    for i in range(NT):
                        for j in range(NT):
                            done = block(i, j)
                        done.then_inc(pt_ready, 1)

            def attend(b, c, steps):
                p = b.parity
                for step in steps:
                    i, n = divmod(step, 3)
                    if step == 0:
                        if c == 0 and is_at_most(b, B - 2):
                            pe.wait_ge(kl_saved, count(b.plus(1), 1, 1))
                        if is_at_least(b, 1):
                            pe.wait_ge(out_saved, count(b.plus(-1), CK, c + 1))
                    if c == 0 and n == 0:
                        pe.wait_ge(pth_saved, count(b, NT, i + 1))
                    if c == 0 and n == 2:
                        pe.wait_ge(ptl_saved, count(b, NT, i + 1))
                    v, pt = ((v_h, pt_h), (v_l, pt_h), (v_h, pt_l))[n]
                    last = nc.tensor.matmul(pv_ps[c][:], v[p][:, i, c * P:(c + 1) * P], pt[:, i, :],
                                            start=(step == 0), stop=(step == 3 * NT - 1))
                if 3 * NT - 1 in steps:
                    last.then_inc(pv_ready, 1)

            def finish(a, b):
                attend(b, 0, range(0, 5))
                product_t1(a)
                attend(b, 0, range(5, 9))
                product_wy(a, 0)
                product_wy(a, 1)
                attend(b, 0, range(9, 3 * NT))
                attend(b, 1, range(0, 2))
                project_q(a)
                attend(b, 1, range(2, 8))
                stack_q(a)
                attend(b, 1, range(8, 3 * NT))

            def slot(b, layer0, layer1):
                a = b.plus(1)
                if not layer1:
                    for j in range(NT):
                        project_pgv(a, j)
                    project_theta(a)
                    transpose_ww()
                    product_mt(a)
                    project_k(a)
                    product_t1(a)
                    product_wy(a, 0)
                    product_wy(a, 1)
                    project_k(a.plus(1))
                    project_q(a)
                    project_pgv(a.plus(1), 0)
                    stack_q(a)
                    project_pgv(a.plus(1), 1)
                elif is_second(a):
                    scores(b)
                    project_pgv(a, 2)
                    project_pgv(a, 3)
                    project_theta(a)
                    product_mt(a)
                    transpose_probs(b, False)
                    finish(a, b)
                elif layer0:
                    scores(b)
                    project_pgv(a, 0)
                    project_pgv(a, 1)
                    project_k(a)
                    project_pgv(a, 2)
                    project_pgv(a, 3)
                    if is_last_but_one(b):
                        project_theta(a)
                        product_mt(a)
                        transpose_probs(b, False)
                        product_t1(a)
                        attend(b, 0, range(0, 4))
                        product_wy(a, 0)
                        product_wy(a, 1)
                        attend(b, 0, range(4, 10))
                        project_q(a)
                        attend(b, 0, range(10, 3 * NT))
                        attend(b, 1, range(0, 4))
                        stack_q(a)
                        attend(b, 1, range(4, 8))
                    else:
                        transpose_probs(b, False)
                        project_theta(a)
                        product_mt(a)
                        finish(a, b)
                else:
                    scores(b)
                    attend(b.plus(-1), 1, range(8, 3 * NT))
                    for _ in range(KEEP_WARM):
                        nc.tensor.matmul(ring_ps[0][:], warm[:, 0:P], warm[:], start=True, stop=True)
                    transpose_probs(b, True)
                    attend(b, 0, range(3 * NT))
                    attend(b, 1, range(3 * NT))

            run_slots(pe, slot)


def pack_vectors(C, CI, D, theta_b, bq, bk, over_c):
    import numpy as np

    cols = [theta_b.reshape(CI, 1), np.concatenate([bq] * (P // D)).reshape(P, 1),
            np.concatenate([bk] * (P // D)).reshape(P, 1)]
    cols += [v.reshape(C // P, P).T for v in over_c]
    return np.ascontiguousarray(np.concatenate(cols, axis=1))


def kernel(**inputs):
    import numpy as np
    import concourse.bacc as bacc
    from concourse.bass_utils import run_bass_kernel_spmd

    a = {k: np.asarray(v) for k, v in inputs.items()}
    B, C, N = a["x"].shape
    CI, D = a["L0_xattn_theta_w"].shape[0], a["L1_xattn_Wq"].shape[0]
    def rows_of(w):
        return w.reshape(C // P, P, -1).transpose(1, 0, 2).reshape(P, -1)

    vectors = pack_vectors(C, CI, D, a["L0_xattn_theta_b"], a["L1_xattn_bq"], a["L1_xattn_bk"],
                           [a["L1_xattn_bv"], a["L0_xattn_w_b"], a["L0_xattn_bn_gamma"],
                            a["L0_xattn_bn_beta"], a["L0_xattn_bn_mean"], a["L0_xattn_bn_var"]])
    b_pg = np.concatenate([a["L0_xattn_phi_b"], a["L0_xattn_g_b"]])
    arrays = {
        "x_dram": a["x"],
        "ctx_dram": a["ctx_2048"],
        "vectors_dram": vectors,
        "w_pgv_dram": np.concatenate([a["L0_xattn_phi_w"].T, a["L0_xattn_g_w"].T, a["L1_xattn_Wv"].T], axis=1),
        "w_pack_a_dram": np.concatenate([rows_of(np.tile(a["L1_xattn_Wk"].T, (1, P // D))), np.broadcast_to(b_pg, (P, 2 * CI)),
                                         np.eye(P, dtype=np.float32)], axis=1),
        "w_pack_b_dram": np.concatenate([rows_of(a["L0_xattn_theta_w"].T), rows_of(a["L0_xattn_w_w"]),
                                         rows_of(a["L1_xattn_Wq"].T)], axis=1),
    }
    arrays = {k: np.ascontiguousarray(v) for k, v in arrays.items()}
    nc = bacc.Bacc("TRN2", target_bir_lowering=False, num_devices=1)
    args = [nc.dram_tensor(k, v.shape, mybir.dt.from_np(v.dtype), kind="ExternalInput").ap() for k, v in arrays.items()]
    out = nc.dram_tensor("out_dram", (B, C, N), F32, kind="ExternalOutput").ap()
    xattn_kernel(nc, *args, CI, D, out)
    r = run_bass_kernel_spmd(nc, [arrays], core_ids=[0])
    return r.results[0]["out_dram"]
```
